# Optimizing a Trainium2 kernel written in Bass

```python
import numpy as np
import jax
import jax.numpy as jnp

def _softmax(x, axis=-1):
    return jax.nn.softmax(x, axis=axis)

def _gelu(x):
    return jax.nn.gelu(x, approximate=True)

def _silu(x):
    return jax.nn.silu(x)

def _sigmoid(x):
    return jax.nn.sigmoid(x)

def _layernorm(x, axis=-1, eps=1e-05):
    m = jnp.mean(x, axis=axis, keepdims=True)
    v = jnp.var(x, axis=axis, keepdims=True)
    return (x - m) / jnp.sqrt(v + eps)

def _scatter_add(tgt, idx, src, axis=0):
    return tgt.at[idx].add(src)

def _segment_sum(src, seg, n):
    return jax.ops.segment_sum(src, seg, n)
kernel_name = 'mk_dlrm_tower_d1_rec_r8_11a2b3'

def setup_inputs(seed: int=0):
    np.random.seed(seed)
    _w = jnp.asarray

    def _rec_inputs():
        import jax
        import jax.numpy as jnp
        _tk = jax.random.key(seed)
        ids = jnp.stack([jax.random.randint(jax.random.fold_in(_tk, 200 + f), (512,), 0, v, jnp.int32) for f, v in enumerate([1000, 1250, 1000, 12500, 1000, 1000, 1250, 1000, 12500, 125000, 1000, 1000, 12500, 1000, 1250, 1000, 1250, 1000, 1000, 12500, 12500, 1250, 1000, 1000, 1250, 1000])], axis=1)
        tbl_0 = 0.05 * jax.random.normal(jax.random.fold_in(_tk, 500 + 0), (1000, 128), jnp.float32)
        tbl_1 = 0.05 * jax.random.normal(jax.random.fold_in(_tk, 500 + 1), (1250, 128), jnp.float32)
        tbl_2 = 0.05 * jax.random.normal(jax.random.fold_in(_tk, 500 + 2), (1000, 128), jnp.float32)
        tbl_3 = 0.05 * jax.random.normal(jax.random.fold_in(_tk, 500 + 3), (12500, 128), jnp.float32)
        tbl_4 = 0.05 * jax.random.normal(jax.random.fold_in(_tk, 500 + 4), (1000, 128), jnp.float32)
        tbl_5 = 0.05 * jax.random.normal(jax.random.fold_in(_tk, 500 + 5), (1000, 128), jnp.float32)
        tbl_6 = 0.05 * jax.random.normal(jax.random.fold_in(_tk, 500 + 6), (1250, 128), jnp.float32)
        tbl_7 = 0.05 * jax.random.normal(jax.random.fold_in(_tk, 500 + 7), (1000, 128), jnp.float32)
        tbl_8 = 0.05 * jax.random.normal(jax.random.fold_in(_tk, 500 + 8), (12500, 128), jnp.float32)
        tbl_9 = 0.05 * jax.random.normal(jax.random.fold_in(_tk, 500 + 9), (125000, 128), jnp.float32)
        tbl_10 = 0.05 * jax.random.normal(jax.random.fold_in(_tk, 500 + 10), (1000, 128), jnp.float32)
        tbl_11 = 0.05 * jax.random.normal(jax.random.fold_in(_tk, 500 + 11), (1000, 128), jnp.float32)
        tbl_12 = 0.05 * jax.random.normal(jax.random.fold_in(_tk, 500 + 12), (12500, 128), jnp.float32)
        tbl_13 = 0.05 * jax.random.normal(jax.random.fold_in(_tk, 500 + 13), (1000, 128), jnp.float32)
        tbl_14 = 0.05 * jax.random.normal(jax.random.fold_in(_tk, 500 + 14), (1250, 128), jnp.float32)
        tbl_15 = 0.05 * jax.random.normal(jax.random.fold_in(_tk, 500 + 15), (1000, 128), jnp.float32)
        tbl_16 = 0.05 * jax.random.normal(jax.random.fold_in(_tk, 500 + 16), (1250, 128), jnp.float32)
        tbl_17 = 0.05 * jax.random.normal(jax.random.fold_in(_tk, 500 + 17), (1000, 128), jnp.float32)
        tbl_18 = 0.05 * jax.random.normal(jax.random.fold_in(_tk, 500 + 18), (1000, 128), jnp.float32)
        tbl_19 = 0.05 * jax.random.normal(jax.random.fold_in(_tk, 500 + 19), (12500, 128), jnp.float32)
        tbl_20 = 0.05 * jax.random.normal(jax.random.fold_in(_tk, 500 + 20), (12500, 128), jnp.float32)
        tbl_21 = 0.05 * jax.random.normal(jax.random.fold_in(_tk, 500 + 21), (1250, 128), jnp.float32)
        tbl_22 = 0.05 * jax.random.normal(jax.random.fold_in(_tk, 500 + 22), (1000, 128), jnp.float32)
        tbl_23 = 0.05 * jax.random.normal(jax.random.fold_in(_tk, 500 + 23), (1000, 128), jnp.float32)
        tbl_24 = 0.05 * jax.random.normal(jax.random.fold_in(_tk, 500 + 24), (1250, 128), jnp.float32)
        tbl_25 = 0.05 * jax.random.normal(jax.random.fold_in(_tk, 500 + 25), (1000, 128), jnp.float32)
        _rk = jax.random.fold_in(_tk, 7)
        r_dense = -0.000520686 + 1.00062 * jax.random.normal(jax.random.fold_in(_rk, 101), (512, 128), jnp.float32)
        W_top1 = 0.0456912 * jax.random.normal(jax.random.fold_in(_tk, 801), (479, 512), jnp.float32)
        W_top2 = 0.0441942 * jax.random.normal(jax.random.fold_in(_tk, 802), (512, 256), jnp.float32)
        W_top3 = 0.0625 * jax.random.normal(jax.random.fold_in(_tk, 803), (256, 1), jnp.float32)
        b_top1 = jnp.zeros((512,), jnp.float32)
        b_top2 = jnp.zeros((256,), jnp.float32)
        return (r_dense, ids, tbl_0, tbl_1, tbl_2, tbl_3, tbl_4, tbl_5, tbl_6, tbl_7, tbl_8, tbl_9, tbl_10, tbl_11, tbl_12, tbl_13, tbl_14, tbl_15, tbl_16, tbl_17, tbl_18, tbl_19, tbl_20, tbl_21, tbl_22, tbl_23, tbl_24, tbl_25, W_top1, b_top1, W_top2, b_top2, W_top3)
    r_dense, ids, tbl_0, tbl_1, tbl_2, tbl_3, tbl_4, tbl_5, tbl_6, tbl_7, tbl_8, tbl_9, tbl_10, tbl_11, tbl_12, tbl_13, tbl_14, tbl_15, tbl_16, tbl_17, tbl_18, tbl_19, tbl_20, tbl_21, tbl_22, tbl_23, tbl_24, tbl_25, W_top1, b_top1, W_top2, b_top2, W_top3 = _rec_inputs()

    def _L0_rec_setup():
        import jax, jax.numpy as jnp
        import numpy as np
        B, NUM_EMBS, D = (2048, 26, 128)
        key = jax.random.key(seed)
        k1, k2 = jax.random.split(key)
        dense = jax.random.normal(k1, (B, D), dtype=jnp.float32)
        embs = jax.random.normal(k2, (B, NUM_EMBS, D), dtype=jnp.float32)
        return {'dense': dense, 'embs': embs}
    _L0_rec_all = _L0_rec_setup()
    _L0_rec_in = {k: v for k, v in _L0_rec_all.items() if k in ()}
    del _L0_rec_all
    return {'r_dense': r_dense, 'ids': ids, 'tbl_0': tbl_0, 'tbl_1': tbl_1, 'tbl_2': tbl_2, 'tbl_3': tbl_3, 'tbl_4': tbl_4, 'tbl_5': tbl_5, 'tbl_6': tbl_6, 'tbl_7': tbl_7, 'tbl_8': tbl_8, 'tbl_9': tbl_9, 'tbl_10': tbl_10, 'tbl_11': tbl_11, 'tbl_12': tbl_12, 'tbl_13': tbl_13, 'tbl_14': tbl_14, 'tbl_15': tbl_15, 'tbl_16': tbl_16, 'tbl_17': tbl_17, 'tbl_18': tbl_18, 'tbl_19': tbl_19, 'tbl_20': tbl_20, 'tbl_21': tbl_21, 'tbl_22': tbl_22, 'tbl_23': tbl_23, 'tbl_24': tbl_24, 'tbl_25': tbl_25, 'W_top1': W_top1, 'b_top1': b_top1, 'W_top2': W_top2, 'b_top2': b_top2, 'W_top3': W_top3}

def reference(r_dense, ids, tbl_0, tbl_1, tbl_2, tbl_3, tbl_4, tbl_5, tbl_6, tbl_7, tbl_8, tbl_9, tbl_10, tbl_11, tbl_12, tbl_13, tbl_14, tbl_15, tbl_16, tbl_17, tbl_18, tbl_19, tbl_20, tbl_21, tbl_22, tbl_23, tbl_24, tbl_25, W_top1, b_top1, W_top2, b_top2, W_top3):
    import jax
    import jax.numpy as jnp

    def _L0_rec_ref(dense, embs):
        import jax, jax.numpy as jnp
        import numpy as np
        B, NUM_EMBS, D = (2048, 26, 128)
        T = jnp.concatenate([dense[:, None, :], embs], axis=1)
        N = T.shape[1]
        Z = jnp.einsum('bnd,bmd->bnm', T, T)
        iu0, iu1 = jnp.triu_indices(N, k=1)
        return Z[:, iu0, iu1]
    e = jnp.stack([tbl_0[ids[:, 0]], tbl_1[ids[:, 1]], tbl_2[ids[:, 2]], tbl_3[ids[:, 3]], tbl_4[ids[:, 4]], tbl_5[ids[:, 5]], tbl_6[ids[:, 6]], tbl_7[ids[:, 7]], tbl_8[ids[:, 8]], tbl_9[ids[:, 9]], tbl_10[ids[:, 10]], tbl_11[ids[:, 11]], tbl_12[ids[:, 12]], tbl_13[ids[:, 13]], tbl_14[ids[:, 14]], tbl_15[ids[:, 15]], tbl_16[ids[:, 16]], tbl_17[ids[:, 17]], tbl_18[ids[:, 18]], tbl_19[ids[:, 19]], tbl_20[ids[:, 20]], tbl_21[ids[:, 21]], tbl_22[ids[:, 22]], tbl_23[ids[:, 23]], tbl_24[ids[:, 24]], tbl_25[ids[:, 25]]], axis=1)
    z = _L0_rec_ref(r_dense, e)
    z = z.reshape(z.shape[0], -1)
    h = jnp.concatenate([z, r_dense], axis=1)
    h = jnp.maximum(h @ W_top1 + b_top1, 0.0)
    h = jnp.maximum(h @ W_top2 + b_top2, 0.0)
    y = h @ W_top3
    return y

_drawn_inputs = setup_inputs


def setup_inputs(seed=0):
    import zlib

    import numpy as np

    out = dict(_drawn_inputs(seed))
    spreads = {'b_top1': (0.0, 0.1), 'b_top2': (0.0, 0.1)}
    factors = {}
    for name, (base, spread) in spreads.items():
        noise = np.random.default_rng([zlib.crc32(name.encode()), seed]).standard_normal(out[name].shape)
        drawn = base * np.exp(spread * noise) if base else spread * noise
        out[name] = jnp.asarray(drawn.astype(out[name].dtype))
    for name, factor in factors.items():
        out[name] = (out[name] * factor).astype(out[name].dtype)
    return out
```

```python
from contextlib import ExitStack

import concourse.bass as bass
from concourse import mybir

F32 = mybir.dt.float32
I32 = mybir.dt.int32
ALU = mybir.AluOpType
ACT = mybir.ActivationFunctionType

P = 128


def tower_program(nc, r_dense, ids, tables, W_top1, b_top1, W_top2, b_top2, W_top3, out):
    B, D = r_dense.shape
    NT = len(tables)
    NF = NT + 1
    H1 = W_top1.shape[1]
    H2 = W_top2.shape[1]
    TILES = B // P
    QUAD = 32
    NG = P // QUAD
    NK = -(-NT // NG)
    NPAIR = NF * (NF - 1) // 2
    SAMP = 2
    PER = 4
    GROUPS = [list(range(a, min(a + PER, NF))) for a in range(0, NF, PER)]
    NGR = len(GROUPS)
    BLK = 16
    BATCHES = P // (SAMP * BLK)
    PITCH = 64
    LEN = P * NF
    M1 = H1 // P
    M2 = H2 // P
    assert D == P and NPAIR + D == W_top1.shape[0] and SAMP * NF <= PITCH

    def first_pair(n):
        return n * (NF - 1) - n * (n - 1) // 2

    with ExitStack() as ctx:
        def sb(name, shape, dt=F32):
            return ctx.enter_context(nc.sbuf_tensor("sb_" + name, shape, dt))

        def psum(name, shape):
            return ctx.enter_context(nc.psum_tensor("ps_" + name, shape, F32))

        def sem(name):
            return ctx.enter_context(nc.semaphore(name))

        ids_sb = sb("ids", [P, TILES, NT], I32)
        dense_sb = sb("dense", [P, TILES, D])
        rows = sb("rows", [P, TILES, NT, D])
        ident = sb("ident", [P, P])
        feats = sb("feats", [P, TILES, LEN + 8])
        pairs = sb("pairs", [P, NK, B])
        dense_t = sb("dense_t", [P, B])
        w1 = sb("w1", [P, NK + 1, H1])
        w2 = sb("w2", [P, M1, H2])
        w3 = sb("w3", [P, M2])
        b1 = sb("b1", [P, M1])
        b2 = sb("b2", [P, M2])
        h1 = sb("h1", [P, M1, P])
        h2 = sb("h2", [P, M2, P])
        y_sb = sb("y", [1, B])

        turned_ps = psum("turned", [P, 2, PER, P])
        prod_ps = psum("prod", [P, 2, BLK, PITCH])
        h1_ps = psum("h1", [P, M1, P])
        h2_ps = psum("h2", [P, 4, P])

        ids_in = sem("ids_in")
        dense_in = sem("dense_in")
        rows_in = [[sem(f"rows_in_{t}_{q}") for q in range(NGR)] for t in range(TILES)]
        w1_cleared = sem("w1_cleared")
        w1_in = sem("w1_in")
        w2_in = sem("w2_in")
        w3_in = sem("w3_in")
        bias_in = sem("bias_in")
        ident_zero = sem("ident_zero")
        ident_ready = sem("ident_ready")
        pairs_cleared = sem("pairs_cleared")
        turned = sem("turned")
        feats_by_dve = sem("feats_by_dve")
        feats_by_act = sem("feats_by_act")
        prods = sem("prods")
        pairs_by_dve = sem("pairs_by_dve")
        pairs_by_act = sem("pairs_by_act")
        h1_summed = sem("h1_summed")
        h1_ready = sem("h1_ready")
        h2_summed = sem("h2_summed")
        h2_ready = sem("h2_ready")
        y_summed = sem("y_summed")
        y_ready = sem("y_ready")
        out_done = sem("out_done")

        block = ctx.enter_context(nc.Block())

        n_w1 = NT + 1

        def stored(at, odd):
            t, q = divmod(at, NGR)
            return t * (NGR // 2 if odd else (NGR + 1) // 2) + (q + 1) // 2 + (0 if odd else (q + 1) % 2)

        def feats_view(t):
            return feats[:, t, 0:LEN].rearrange("p (b n) -> p n b", n=NF)

        def pairs_step(copy, s, t, b, wait):
            for g in range(NG):
                k = len(range(g, NT, NG))
                src = prod_ps[QUAD * s:QUAD * s + NF, b % 2, :, s * NF + g:s * NF + NT:NG]
                c = t * P + s * (P // SAMP) + b * BLK
                last = copy(pairs[QUAD * g:QUAD * g + NF, 0:k, c:c + BLK],
                            src.rearrange("m i k -> m k i"))
            return last

        @block.sync
        def _(sp):
            sp.dma_start(ids_sb[:, :, :], ids.rearrange("(t p) f -> p t f", p=P)).then_inc(ids_in, 16)
            sp.dma_start(dense_sb[:, :, :], r_dense.rearrange("(t p) d -> p t d", p=P)).then_inc(dense_in, 16)
            sp.wait_ge(w1_cleared, 1)
            for n in range(NT):
                at = QUAD * (n % NG) + n + 1
                sp.dma_start(w1[at:at + NT - n, n // NG, :],
                             W_top1[first_pair(n):first_pair(n) + NT - n, :]).then_inc(w1_in, 16)
            sp.dma_start(w1[:, NK, :], W_top1[NPAIR:NPAIR + D, :]).then_inc(w1_in, 16)
            sp.dma_start(w2[:, :, :], W_top2.rearrange("(c p) n -> p c n", p=P)).then_inc(w2_in, 16)
            sp.dma_start(w3[:, :], W_top3.rearrange("(c p) n -> p (c n)", p=P), allow_slow_non_contiguous=True).then_inc(w3_in, 16)
            sp.dma_start(b1[:, :], b_top1.rearrange("(c p) -> p c", p=P), allow_slow_non_contiguous=True).then_inc(bias_in, 16)
            sp.dma_start(b2[:, :], b_top2.rearrange("(c p) -> p c", p=P), allow_slow_non_contiguous=True).then_inc(bias_in, 16)
            sp.wait_ge(y_ready, TILES)
            sp.dma_start(out.rearrange("b n -> n b"), y_sb[:, :]).then_inc(out_done, 16)
            sp.wait_ge(out_done, 16)

        @block.gpsimd
        def _(pool):
            pool.memset(ident[:, :], 0.0).then_inc(ident_zero, 1)
            pool.wait_ge(ident_zero, 1)
            pool.affine_select(out=ident[:, :], in_=ident[:, :], compare_op=ALU.not_equal, fill=1.0,
                               base=0, pattern=[[-1, P]], channel_multiplier=1).then_inc(ident_ready, 1)
            pool.wait_ge(ids_in, 16)
            for t in range(TILES):
                for q, group in enumerate(GROUPS):
                    for n in group:
                        if n > 0:
                            pool.indirect_dma_start(
                                rows[:, t, n - 1, :], None, tables[n - 1],
                                bass.IndirectOffsetOnAxis(ids_sb[:, t, n - 1:n], 0)).then_inc(rows_in[t][q], 16)

        @block.vector
        def _(dve):
            dve.memset(w1[:, :, :], 0.0).then_inc(w1_cleared, 1)
            dve.memset(pairs[:, :, :], 0.0).then_inc(pairs_cleared, 1)
            for t in range(TILES):
                for q in range(0, NGR, 2):
                    bank = turned_ps[:, (t * NGR + q) % 2, :, :]
                    dve.wait_ge(turned, t * NGR + q + 1)
                    if q == 0:
                        dve.tensor_copy(dense_t[:, t * P:(t + 1) * P].rearrange("p (s i) -> p s i", s=SAMP),
                                        bank[:, 0, :].rearrange("p (i s) -> p s i", s=SAMP))
                    g = GROUPS[q]
                    dve.tensor_copy(feats_view(t)[:, g[0]:g[-1] + 1, :],
                                    bank[:, 0:len(g), :]).then_inc(feats_by_dve, 1)
                if t == 0:
                    dve.wait_ge(pairs_cleared, 1)
                for b in range(BATCHES):
                    dve.wait_ge(prods, t * BATCHES + b + 1)
                    pairs_step(dve.tensor_copy, 0, t, b, None).then_inc(pairs_by_dve, 1)
                dve.wait_ge(y_summed, t + 1)
                dve.tensor_copy(y_sb[:, t * P:(t + 1) * P].rearrange("o (i s) -> o s i", s=SAMP),
                                h2_ps[0:1, M2, :].rearrange("o (s i) -> o s i", s=SAMP)).then_inc(y_ready, 1)

        @block.scalar
        def _(act):
            for t in range(TILES):
                for q in range(1, NGR, 2):
                    g = GROUPS[q]
                    act.wait_ge(turned, t * NGR + q + 1)
                    act.copy(feats_view(t)[:, g[0]:g[-1] + 1, :],
                             turned_ps[:, (t * NGR + q) % 2, 0:len(g), :]).then_inc(feats_by_act, 1)
                if t == 0:
                    act.wait_ge(pairs_cleared, 1)
                for b in range(BATCHES):
                    act.wait_ge(prods, t * BATCHES + b + 1)
                    pairs_step(act.copy, 1, t, b, None).then_inc(pairs_by_act, 1)
                act.wait_ge(bias_in, 32)
                act.wait_ge(h1_summed, t + 1)
                for c in range(M1):
                    last = act.activation(h1[:, c, :], h1_ps[:, c, :], ACT.Relu, bias=b1[:, c:c + 1])
                last.then_inc(h1_ready, 1)
                act.wait_ge(h2_summed, t + 1)
                for c in range(M2):
                    last = act.activation(h2[:, c, :], h2_ps[:, c, :], ACT.Relu, bias=b2[:, c:c + 1])
                last.then_inc(h2_ready, 1)

        @block.tensor
        def _(pe):
            pe.wait_ge(ident_ready, 1)
            pe.wait_ge(dense_in, 16)
            for t in range(TILES):
                for q, group in enumerate(GROUPS):
                    pe.wait_ge(rows_in[t][q], 16 * len([n for n in group if n > 0]))
                    at = t * NGR + q
                    if at >= 2:
                        pe.wait_ge(feats_by_dve, stored(at - 2, False))
                        if stored(at - 2, True):
                            pe.wait_ge(feats_by_act, stored(at - 2, True))
                    for i, n in enumerate(group):
                        src = dense_sb[:, t, :] if n == 0 else rows[:, t, n - 1, :]
                        last = pe.transpose(turned_ps[:, at % 2, i, :], src, ident[:, :])
                    last.then_inc(turned, 1)
                pe.wait_ge(feats_by_dve, stored(t * NGR + NGR - 1, False))
                pe.wait_ge(feats_by_act, stored(t * NGR + NGR - 1, True))
                for b in range(BATCHES):
                    done = t * BATCHES + b
                    if done >= 2:
                        pe.wait_ge(pairs_by_dve, done - 1)
                        pe.wait_ge(pairs_by_act, done - 1)
                    for i in range(BLK):
                        at = (b * BLK + i) * SAMP * NF
                        two = feats[:, t, at:at + SAMP * NF]
                        for s in range(SAMP):
                            last = pe.matmul(prod_ps[QUAD * s:QUAD * s + NF, b % 2, i, 0:SAMP * NF],
                                             two[:, s * NF:(s + 1) * NF], two, start=True, stop=True)
                    last.then_inc(prods, 1)
                pe.wait_ge(pairs_by_dve, (t + 1) * BATCHES)
                pe.wait_ge(pairs_by_act, (t + 1) * BATCHES)
                if t == 0:
                    pe.wait_ge(w1_in, 16 * n_w1)
                    pe.wait_ge(w2_in, 16)
                    pe.wait_ge(w3_in, 16)
                if t >= 1:
                    pe.wait_ge(h1_ready, t)
                for c in range(M1):
                    for k in range(NK + 1):
                        part = pairs[:, k, t * P:(t + 1) * P] if k < NK else dense_t[:, t * P:(t + 1) * P]
                        last = pe.matmul(h1_ps[:, c, :], w1[:, k, c * P:(c + 1) * P], part,
                                         start=(k == 0), stop=(k == NK))
                last.then_inc(h1_summed, 1)
                pe.wait_ge(h1_ready, t + 1)
                if t >= 1:
                    pe.wait_ge(h2_ready, t)
                    pe.wait_ge(y_ready, t)
                for c in range(M2):
                    for k in range(M1):
                        last = pe.matmul(h2_ps[:, c, :], w2[:, k, c * P:(c + 1) * P], h1[:, k, :],
                                         start=(k == 0), stop=(k == M1 - 1))
                last.then_inc(h2_summed, 1)
                pe.wait_ge(h2_ready, t + 1)
                for k in range(M2):
                    last = pe.matmul(h2_ps[0:1, M2, :], w3[:, k:k + 1], h2[:, k, :],
                                     start=(k == 0), stop=(k == M2 - 1))
                last.then_inc(y_summed, 1)


def kernel(**inputs):
    import numpy as np
    import concourse.bacc as bacc
    from concourse.bass_utils import run_bass_kernel_spmd

    nc = bacc.Bacc("TRN2", target_bir_lowering=False, num_devices=1)
    arrays, aps = {}, {}
    for name, value in inputs.items():
        a = np.ascontiguousarray(value)
        arrays[f"in_{name}"] = a
        aps[name] = nc.dram_tensor(f"in_{name}", a.shape, mybir.dt.from_np(a.dtype), kind="ExternalInput").ap()
    batch = inputs["r_dense"].shape[0]
    out = nc.dram_tensor("out_y", (batch, 1), F32, kind="ExternalOutput").ap()
    tables = [aps[f"tbl_{i}"] for i in range(inputs["ids"].shape[1])]
    tower_program(nc, aps["r_dense"], aps["ids"], tables, aps["W_top1"], aps["b_top1"],
                  aps["W_top2"], aps["b_top2"], aps["W_top3"], out)
    r = run_bass_kernel_spmd(nc, [arrays], core_ids=[0])
    return r.results[0]["out_y"]
```

```python
from contextlib import ExitStack

import concourse.bass as bass
from concourse import mybir

F32 = mybir.dt.float32
F32R = mybir.dt.float32r
I32 = mybir.dt.int32
ALU = mybir.AluOpType
ACT = mybir.ActivationFunctionType

P = 128
QUAD = 32
SLOTS = 28
ROWS_PER_PART = 8
CHOSEN_FROM = {0: 3, 1: 4, 2: 2}

PACK_CUT = 2
PACK = [
    (0, 14, [(14, 1, 0), (14, 0, 1)]),
    (0, 7, [(2, 14, 14), (7, 1, 0), (7, 0, 1)]),
    (0, 4, [(4, 7, 7), (4, 1, 0), (3, 0, 1)]),
    (0, 2, [(4, 7, 7), (2, 1, 0), (2, 0, 1)]),
    (0, 1, [(4, 7, 7), (2, 2, 2)]),
    (4, 5, [(4, 7, 7), (2, 0, 1)]),
    (5, 6, [(4, 7, 7)]),
]


def pack_order():
    order = []
    for n0, m0, dims in PACK:
        at = [(n0, m0)]
        for count, dn, dm in dims:
            at = [(n + i * dn, m + i * dm) for n, m in at for i in range(count)]
        order += at
    assert sorted(order) == [(n, m) for n in range(SLOTS) for m in range(n + 1, SLOTS)]
    return order


ORDER = """
I S0 L0 S1 H0.0 T0.0 E0.0a L1 C0.0 H0.1 T0.1 H1.0 C0.1 E0.1a E0a H1.1 S2 C1.0 T0.2 L2 C1.1
E0.2a H2.0 E1a S3 T0.3 H2.1 C2.0 E0.3a L3 C2.1 H3.0 T0.4 E2a E0.4a H3.1 S4 C3.0 L4 C3.1 H4.0
T0.5 E3a S5 E0.5d C4.0 X0 H4.1 H5.0 L5 T1.0 C4.1 E1.0a V0 E4a H5.1 H6.0 S6 T1.1 C5.0 Q0.1a
Q0.0a E1.1a L6 C5.1 H6.1 K0 E5a T1.2 W0a C6.0 E1.2a S7 H7.0 A0.0 L7 A0.1 R0.0 H7.1 C6.1 R0.1
B0 E6a H8.0 S8 T1.3 U0.0 T1.4 U0.1 E1.3a Y0 E1.4d T2.0 L8 E2.0a Z0a X1 C7.0 V1 C7.1 H8.1
Q1.0a C8.0 Q1.1a E7a K1 C8.1 W1a T2.1 E8d A1.0 E2.1d A1.1 R1.0 T2.2 R1.1 T2.3 E2.2d B1 E2.3a
T2.4 U1.0 U1.1 E2.4d Y1 X2 Z1a T3.0 V2 T3.1 E3.0a E3.1a Q2.0d Q2.1d K2 W2a A2.0 A2.1 R2.0
T3.2 R2.1 E3.2a T3.3 B2 U2.0 U2.1 E3.3d T3.4 V3 Y2 E3.4a Z2d X3 Q3.1a Q3.0d K3 W3a A3.0 A3.1
R3.0 R3.1 B3 U3.0 Y3 U3.1 Z3a
"""

STEP_NAMES = {
    "I": "ids", "S": "high", "L": "low", "H": "hot", "C": "choose", "T": "turn", "E": "empty",
    "X": "products", "V": "spread", "Q": "packing", "K": "pack", "W": "pairs", "A": "layer1",
    "R": "relu1", "B": "layer2", "U": "relu2", "Y": "layer3", "Z": "result",
}


def read_order(text):
    steps = []
    for word in text.split():
        who = {"a": "act", "d": "dve"}.get(word[-1])
        numbers = word[1:-1] if who else word[1:]
        steps.append((STEP_NAMES[word[0]], tuple(int(n) for n in numbers.split(".") if n), who))
    return steps


def slot_plan(table_rows):
    fit = [f for f, r in enumerate(table_rows) if r % ROWS_PER_PART == 0 and r // ROWS_PER_PART <= P]
    chosen, start = [], []
    for t, count in sorted(CHOSEN_FROM.items()):
        chosen += fit[len(chosen):len(chosen) + count]
        start += [t] * count
    assert len(chosen) == sum(CHOSEN_FROM.values())
    rest = [f for f in range(len(table_rows)) if f not in chosen]
    slots = [0] + [f + 1 for f in rest + chosen[::-1]]
    return slots, chosen, start


def w1_rows(table_rows, depth):
    slots, _, _ = slot_plan(table_rows)
    nf = len(slots)
    rows = []
    for n, m in pack_order():
        if max(n, m) < nf:
            a, b = sorted((slots[n], slots[m]))
            rows.append(a * (nf - 1) - a * (a - 1) // 2 + b - a - 1)
        else:
            rows.append(0)
    rows += [0] * (-len(rows) % P)
    return rows + [nf * (nf - 1) // 2 + d for d in range(depth)]


def tower_program(nc, r_dense, ids, tables, w1_laid, b_top1, W_top2, b_top2, W_top3, out):
    B, D = r_dense.shape
    NT = len(tables)
    TILES = B // P
    _, K1, H1 = w1_laid.shape
    H2 = W_top2.shape[1]
    M1, M2 = H1 // P, H2 // P
    NP = SLOTS * (SLOTS - 1) // 2
    PK = -(-NP // P)
    slots, chosen, start = slot_plan([t.shape[0] for t in tables])
    NF = len(slots)
    NCH = len(chosen)
    CR = tables[chosen[0]].shape[0] // ROWS_PER_PART
    CHUNKS = ROWS_PER_PART
    LEN = P * SLOTS
    HALF = QUAD // 2
    assert D == P and NF < SLOTS and K1 == PK + 1 and M1 == 4 and M2 == 2

    def gathered(t):
        return NF - sum(1 for s in start if s <= t)

    def groups(t):
        return [list(range(a, min(a + 4, gathered(t)))) for a in range(0, gathered(t), 4)]

    STEPS = read_order(ORDER)
    turns = [n for name, n, _ in STEPS if name == "turn"]
    items = [n if name == "turn" else n[:1] for name, n, _ in STEPS
             if name == "turn" or (name == "choose" and n[1] == 0)]
    emptiers = [(n, who) for name, n, who in STEPS if name == "empty"]
    packers = [(n, who) for name, n, who in STEPS if name == "packing"]

    def count_of(jobs, n):
        who = dict(jobs)[n]
        own = [m for m, w in jobs if w == who]
        return who, own.index(n) + 1

    def items_of(t):
        return [n for n in items if (len(n) == 2 and n[0] == t) or (len(n) == 1 and start[n[0]] <= t)]

    def width(j):
        return (TILES - start[j]) * P

    with ExitStack() as ctx:
        def sb(name, shape, dt=F32):
            return ctx.enter_context(nc.sbuf_tensor("sb_" + name, shape, dt))

        def psum(name, shape):
            return ctx.enter_context(nc.psum_tensor("ps_" + name, shape, F32))

        def sem(name):
            return ctx.enter_context(nc.semaphore(name))

        TABLES_AHEAD = 3
        SPLITS = 2
        ONE_HOTS = 12
        ids_sb = sb("ids", [P, TILES, NT], I32)
        ids_f = sb("ids_f", [P, TILES, NT])
        ids_t = sb("ids_t", [NT, B], F32R)
        pick = sb("pick", [NT, NCH, P], F32R)
        part_no = sb("part_no", [1, P], I32)
        minus_8p = sb("minus_8p", [1, P], F32R)
        ones = sb("ones", [1, B], F32R)
        dense_sb = sb("dense", [P, TILES, D])
        rows = sb("rows", [P, sum(gathered(t) - 1 for t in range(TILES)), D])
        ident = sb("ident", [P, P])
        table = sb("table", [CR, TABLES_AHEAD, CHUNKS, D])
        table_hi = sb("table_hi", [CR, SPLITS, CHUNKS, D], F32R)
        table_lo = sb("table_lo", [CR, SPLITS, CHUNKS, D], F32R)
        one_hot = sb("one_hot", [CR, ONE_HOTS, B], F32R)
        feats = sb("feats", [P, TILES, LEN + 8])
        spread = sb("spread", [P, NF, QUAD])
        packed = sb("packed", [P, PK * P])
        pairs = sb("pairs", [P, 2, PK, P])
        dense_t = sb("dense_t", [P, B])
        w1 = sb("w1", [P, K1, H1])
        w2 = sb("w2", [P, M1, H2])
        w3 = sb("w3", [P, M2])
        b1 = sb("b1", [P, M1])
        b2 = sb("b2", [P, M2])
        h1 = sb("h1", [P, M1, P])
        h2 = sb("h2", [P, M2, P])
        y_sb = sb("y", [1, B])

        turned_ps = psum("turned", [P, 2, 4 * P])
        ids_ps = psum("ids", [P, 2, 4 * P])
        prod_ps = psum("prod", [P, 2 * HALF, QUAD])
        pack_ps = psum("pack", [P, 4, P])
        mlp_ps = psum("mlp", [P, 4, P])

        ids_in = sem("ids_in")
        dense_in = sem("dense_in")
        rows_in = {(t, q): sem(f"rows_in_{t}_{q}") for t in range(TILES) for q in range(len(groups(t)))}
        table_in = [sem(f"table_in_{r}") for r in range(TABLES_AHEAD)]
        weights_in = sem("weights_in")
        bias_in = sem("bias_in")
        ident_zero = sem("ident_zero")
        ident_ready = sem("ident_ready")
        part_no_ready = sem("part_no_ready")
        picks_ready = sem("picks_ready")
        blanks_ready = sem("blanks_ready")
        ids_f_ready = sem("ids_f_ready")
        ids_turned = sem("ids_turned")
        ids_t_ready = sem("ids_t_ready")
        ids_spread = sem("ids_spread")
        hi_ready = sem("hi_ready")
        lo_ready = sem("lo_ready")
        one_hot_ready = sem("one_hot_ready")
        one_hot_used = sem("one_hot_used")
        turned = sem("turned")
        emptied = {"dve": sem("emptied_by_dve"), "act": sem("emptied_by_act")}
        prods_ready = sem("prods_ready")
        spread_ready = sem("spread_ready")
        packed_by = {"dve": sem("packed_by_dve"), "act": sem("packed_by_act")}
        packs_turned = sem("packs_turned")
        pairs_ready = sem("pairs_ready")
        h1_summed = sem("h1_summed")
        h1_ready = sem("h1_ready")
        h2_summed = sem("h2_summed")
        h2_ready = sem("h2_ready")
        y_summed = sem("y_summed")
        y_ready = sem("y_ready")
        out_done = sem("out_done")

        block = ctx.enter_context(nc.Block())

        row_at = {}
        for t in range(TILES):
            for s in range(1, gathered(t)):
                row_at[t, s] = len(row_at)

        def feats_of(t):
            return feats[:, t, 0:LEN].rearrange("p (b s) -> p s b", s=SLOTS)

        def empty(copy, wait, n, done_sem):
            bank = turned_ps[:, items.index(n) % 2, :]
            if len(n) == 2:
                t, q = n
                wait(turned, turns.index(n) + 1)
                g = groups(t)[q]
                if q == 0:
                    copy(dense_t[:, t * P:(t + 1) * P], bank[:, 0:P])
                done = copy(feats_of(t)[:, g[0]:g[-1] + 1, :],
                            bank[:, 0:len(g) * P].rearrange("p (s b) -> p s b", b=P))
            else:
                j, = n
                slot = NF - 1 - j
                wait(one_hot_used, CHUNKS * (j + 1))
                dst = feats[:, start[j]:TILES, 0:LEN].rearrange("p t (b s) -> p t b s", s=SLOTS)[:, :, :, slot]
                done = copy(dst, bank[:, 0:width(j)].rearrange("p (t b) -> p t b", b=P))
            done.then_inc(done_sem, 1)

        def packing(copy, wait, t, part, done_sem):
            wait(spread_ready, t + 1)
            if t >= 1:
                wait(packs_turned, t)
            at = 0
            for r, (n0, m0, dims) in enumerate(PACK):
                sizes = [count for count, _, _ in dims]
                total, runs = 1, []
                for count in sizes[::-1]:
                    runs.insert(0, [total, count])
                    total *= count
                if (r >= PACK_CUT) == part:
                    src, dst = spread[:, n0, m0:m0 + 1], packed[:, at:at + total]
                    done = copy(
                        bass.AP(dst.tensor, dst.offset, [list(dst.ap[0])] + runs),
                        bass.AP(src.tensor, src.offset, [list(src.ap[0])] + [
                            [dn * QUAD + dm, count] for count, dn, dm in dims]))
                at += total
            done.then_inc(done_sem, 1)

        def pairs_step(copy, wait, t):
            wait(packs_turned, t + 1)
            if t >= 2:
                wait(h1_summed, 2 * (t - 1))
            copy(pairs[:, t % 2, :, :], pack_ps[:, 0:PK, :]).then_inc(pairs_ready, 1)

        def result_step(copy, wait, t):
            wait(y_summed, t + 1)
            copy(y_sb[:, t * P:(t + 1) * P], mlp_ps[0:1, 3, :]).then_inc(y_ready, 1)

        def either_engine(me, copy, wait, name, n, who):
            if who != me:
                return
            if name == "empty":
                empty(copy, wait, n, emptied[me])
            if name == "packing":
                packing(copy, wait, *n, packed_by[me])
            if name == "pairs":
                pairs_step(copy, wait, *n)
            if name == "result":
                result_step(copy, wait, *n)

        def h1_sum(c):
            return (mlp_ps if c < 2 else pack_ps)[:, c % 2, :]

        def h2_sum(c):
            return (mlp_ps if c < 1 else pack_ps)[:, 2, :]

        def load_table(q, j):
            src = tables[chosen[j]].rearrange("(p c) d -> p c d", c=ROWS_PER_PART)
            cut = CR // 16 * 16
            for a, b in ((0, cut), (cut, CR)):
                q.dma_start(table[a:b, j % TABLES_AHEAD, :, :], src[a:b]).then_inc(table_in[j % TABLES_AHEAD], 16)

        @block.sync
        def _(sp):
            sp.dma_start(ids_sb[:, :, :], ids.rearrange("(t p) f -> p t f", p=P)).then_inc(ids_in, 16)
            load_table(sp, 0)
            sp.dma_start(dense_sb[:, :, :], r_dense.rearrange("(t p) d -> p t d", p=P)).then_inc(dense_in, 16)
            for j in range(1, TABLES_AHEAD):
                load_table(sp, j)
            sp.dma_start(w1[:, :, :], w1_laid).then_inc(weights_in, 16)
            sp.dma_start(w2[:, :, :], W_top2.rearrange("(c p) n -> p c n", p=P)).then_inc(weights_in, 16)
            sp.dma_start(w3[:, :], W_top3.rearrange("(c p) n -> p (c n)", p=P),
                         allow_slow_non_contiguous=True).then_inc(weights_in, 16)
            sp.dma_start(b1[:, :], b_top1.rearrange("(c p) -> p c", p=P),
                         allow_slow_non_contiguous=True).then_inc(bias_in, 16)
            sp.dma_start(b2[:, :], b_top2.rearrange("(c p) -> p c", p=P),
                         allow_slow_non_contiguous=True).then_inc(bias_in, 16)
            for j in range(TABLES_AHEAD, NCH):
                sp.wait_ge(lo_ready, j - TABLES_AHEAD + 1)
                load_table(sp, j)
            sp.wait_ge(y_ready, TILES)
            sp.dma_start(out.rearrange("b n -> n b"), y_sb[:, :]).then_inc(out_done, 16)
            sp.wait_ge(out_done, 16)

        @block.gpsimd
        def _(pool):
            pool.memset(ident[:, :], 0.0).then_inc(ident_zero, 1)
            pool.iota(part_no[:, :], [[1, P]], base=0, channel_multiplier=0).then_inc(part_no_ready, 1)
            pool.wait_ge(ident_zero, 1)
            pool.affine_select(out=ident[:, :], in_=ident[:, :], compare_op=ALU.not_equal, fill=1.0,
                               base=0, pattern=[[-1, P]], channel_multiplier=1).then_inc(ident_ready, 1)
            pool.wait_ge(ids_in, 16)
            for t in range(TILES):
                for q, group in enumerate(groups(t)):
                    for s in group:
                        if s > 0:
                            f = slots[s] - 1
                            pool.indirect_dma_start(
                                rows[:, row_at[t, s], :], None, tables[f],
                                bass.IndirectOffsetOnAxis(ids_sb[:, t, f:f + 1], 0)).then_inc(rows_in[t, q], 16)

        @block.vector
        def _(dve):
            dve.memset(ones[:, :].bitcast(F32), 1.0).then_inc(blanks_ready, 1)
            dve.memset(feats[:, :, 0:LEN].rearrange("p t (b s) -> p t b s", s=SLOTS)[:, :, :, NF:SLOTS],
                       0.0).then_inc(blanks_ready, 1)
            dve.memset(feats[:, :, LEN:LEN + 8], 0.0).then_inc(blanks_ready, 1)
            dve.memset(packed[:, NP:PK * P], 0.0).then_inc(blanks_ready, 1)
            for name, n, who in STEPS:
                if name == "ids":
                    dve.wait_ge(ids_in, 16)
                    dve.tensor_copy(ids_f[:, :, :], ids_sb[:, :, :]).then_inc(ids_f_ready, 1)
                    dve.wait_ge(ids_turned, 1)
                    dve.tensor_copy(ids_t[:, :], ids_ps[0:NT, 0, :]).then_inc(ids_t_ready, 1)
                if name == "low":
                    j, = n
                    dve.wait_ge(hi_ready, j + 1)
                    if j >= SPLITS:
                        dve.wait_ge(one_hot_used, CHUNKS * (j - SPLITS + 1))
                    dve.tensor_tensor(table_lo[:, j % SPLITS, :, :], table[:, j % TABLES_AHEAD, :, :],
                                      table_hi[:, j % SPLITS, :, :], ALU.subtract).then_inc(lo_ready, 1)
                if name == "hot":
                    j, half = n
                    dve.wait_ge(ids_spread, j + 1)
                    for c in range(half * CHUNKS // 2, (half + 1) * CHUNKS // 2):
                        at = j * CHUNKS + c
                        if at >= ONE_HOTS:
                            dve.wait_ge(one_hot_used, at - ONE_HOTS + 1)
                        dve.tensor_scalar(one_hot[:, at % ONE_HOTS, 0:width(j)], ids_ps[0:CR, j % 2, 0:width(j)],
                                          float(c), None, ALU.is_equal).then_inc(one_hot_ready, 1)
                if name == "spread":
                    t, = n
                    dve.wait_ge(prods_ready, t + 1)
                    if t >= 1:
                        for part in range(2):
                            by, count = count_of(packers, (t - 1, part))
                            dve.wait_ge(packed_by[by], count)
                    dve.transpose(spread[:, :, :], prod_ps[:, :, 0:NF].rearrange("p i n -> p n i")).then_inc(spread_ready, 1)
                either_engine("dve", dve.tensor_copy, dve.wait_ge, name, n, who)

        @block.scalar
        def _(act):
            act.wait_ge(part_no_ready, 1)
            act.mul(minus_8p[:, :], part_no[:, :], -float(ROWS_PER_PART)).then_inc(picks_ready, 1)
            act.wait_ge(ident_ready, 1)
            for j in range(NCH):
                act.copy(pick[:, j, :], ident[0:NT, chosen[j]:chosen[j] + 1].to_broadcast([NT, P])).then_inc(picks_ready, 1)
            for name, n, who in STEPS:
                if name == "high":
                    j, = n
                    act.wait_ge(table_in[j % TABLES_AHEAD], 32 * (j // TABLES_AHEAD + 1))
                    if j >= SPLITS:
                        act.wait_ge(one_hot_used, CHUNKS * (j - SPLITS + 1))
                    act.copy(table_hi[:, j % SPLITS, :, :], table[:, j % TABLES_AHEAD, :, :]).then_inc(hi_ready, 1)
                if name == "relu1":
                    t, half = n
                    if t == 0 and half == 0:
                        act.wait_ge(bias_in, 32)
                    act.wait_ge(h1_summed, 2 * t + half + 1)
                    for c in range(2):
                        unit = 2 * half + c
                        done = act.activation(h1[:, unit, :], h1_sum(unit), ACT.Relu, bias=b1[:, unit:unit + 1])
                    done.then_inc(h1_ready, 1)
                if name == "relu2":
                    t, c = n
                    act.wait_ge(h2_summed, 2 * t + c + 1)
                    act.activation(h2[:, c, :], h2_sum(c), ACT.Relu, bias=b2[:, c:c + 1]).then_inc(h2_ready, 1)
                either_engine("act", act.copy, act.wait_ge, name, n, who)

        @block.tensor
        def _(pe):
            def bank_free(i):
                if i >= 2:
                    by, count = count_of(emptiers, items[i - 2])
                    pe.wait_ge(emptied[by], count)

            def spread_ids(j):
                w = width(j)
                pe.matmul(ids_ps[:, j % 2, 0:w], pick[:, j, :], ids_t[:, B - w:B], start=True, stop=False)
                pe.matmul(ids_ps[:, j % 2, 0:w], minus_8p[:, :], ones[:, 0:w],
                          start=False, stop=True).then_inc(ids_spread, 1)

            def layer2_part(c, ks):
                for k in ks:
                    done = pe.matmul(h2_sum(c), w2[:, k, c * P:(c + 1) * P], h1[:, k, :],
                                     start=(k == 0), stop=(k == M1 - 1))
                return done

            for name, n, _ in STEPS:
                if name == "ids":
                    pe.wait_ge(ident_ready, 1)
                    pe.wait_ge(ids_f_ready, 1)
                    for t in range(TILES):
                        done = pe.transpose(ids_ps[0:NT, 0, t * P:(t + 1) * P], ids_f[:, t, :], ident[:, :])
                    done.then_inc(ids_turned, 1)
                    pe.wait_ge(ids_t_ready, 1)
                    pe.wait_ge(picks_ready, 1 + NCH)
                    pe.wait_ge(blanks_ready, 4)
                    spread_ids(0)
                    spread_ids(1)
                if name == "turn":
                    t, q = n
                    i = items.index(n)
                    group = groups(t)[q]
                    if q == 0:
                        pe.wait_ge(dense_in, 16)
                    bank_free(i)
                    pe.wait_ge(rows_in[t, q], 16 * len([s for s in group if s > 0]))
                    for k, s in enumerate(group):
                        src = dense_sb[:, t, :] if s == 0 else rows[:, row_at[t, s], :]
                        done = pe.transpose(turned_ps[:, i % 2, k * P:(k + 1) * P], src, ident[:, :])
                    done.then_inc(turned, 1)
                if name == "choose":
                    j, half = n
                    i = items.index((j,))
                    w = width(j)
                    if half == 0:
                        bank_free(i)
                        pe.wait_ge(lo_ready, j + 1)
                    for c in range(half * CHUNKS // 2, (half + 1) * CHUNKS // 2):
                        at = j * CHUNKS + c
                        pe.wait_ge(one_hot_ready, at + 1)
                        hot = one_hot[:, at % ONE_HOTS, 0:w]
                        pe.matmul(turned_ps[:, i % 2, 0:w], table_hi[:, j % SPLITS, c, :], hot, start=(c == 0), stop=False)
                        pe.matmul(turned_ps[:, i % 2, 0:w], table_lo[:, j % SPLITS, c, :], hot,
                                  start=False, stop=(c == CHUNKS - 1)).then_inc(one_hot_used, 1)
                    if half == 1 and j + 2 < NCH:
                        spread_ids(j + 2)
                if name == "products":
                    t, = n
                    counts = {}
                    for item in items_of(t):
                        by, count = count_of(emptiers, item)
                        counts[by] = max(count, counts.get(by, 0))
                    for by, count in sorted(counts.items()):
                        pe.wait_ge(emptied[by], count)
                    if t >= 1:
                        pe.wait_ge(spread_ready, t)
                    for i in range(QUAD):
                        for quad in range(P // QUAD):
                            at = (quad * QUAD + i) * SLOTS
                            done = pe.matmul(prod_ps[quad * QUAD:(quad + 1) * QUAD, i, 0:NF],
                                             feats[:, t, at:at + QUAD], feats[:, t, at:at + NF],
                                             start=True, stop=True)
                    done.then_inc(prods_ready, 1)
                if name == "pack":
                    t, = n
                    for part in range(2):
                        by, count = count_of(packers, (t, part))
                        pe.wait_ge(packed_by[by], count)
                    if t >= 1:
                        pe.wait_ge(h2_ready, 2 * t)
                    for k in range(PK):
                        done = pe.transpose(pack_ps[:, k, :], packed[:, k * P:(k + 1) * P], ident[:, :])
                    done.then_inc(packs_turned, 1)
                if name == "layer1":
                    t, half = n
                    pe.wait_ge(pairs_ready, t + 1)
                    if half == 0:
                        if t == 0:
                            pe.wait_ge(weights_in, 48)
                        else:
                            pe.wait_ge(y_ready, t)
                    for c in range(2 * half, 2 * half + 2):
                        for k in range(K1):
                            part = pairs[:, t % 2, k, :] if k < PK else dense_t[:, t * P:(t + 1) * P]
                            done = pe.matmul(h1_sum(c), w1[:, k, c * P:(c + 1) * P], part,
                                             start=(k == 0), stop=(k == K1 - 1))
                    done.then_inc(h1_summed, 1)
                if name == "layer2":
                    t, = n
                    pe.wait_ge(h1_ready, 2 * t + 1)
                    layer2_part(0, range(0, 2))
                    pe.wait_ge(h1_ready, 2 * t + 2)
                    layer2_part(0, range(2, M1)).then_inc(h2_summed, 1)
                    layer2_part(1, range(M1)).then_inc(h2_summed, 1)
                if name == "layer3":
                    t, = n
                    for k in range(M2):
                        pe.wait_ge(h2_ready, 2 * t + k + 1)
                        done = pe.matmul(mlp_ps[0:1, 3, :], w3[:, k:k + 1], h2[:, k, :],
                                         start=(k == 0), stop=(k == M2 - 1))
                    done.then_inc(y_summed, 1)


def kernel(**inputs):
    import numpy as np
    import concourse.bacc as bacc
    from concourse.bass_utils import run_bass_kernel_spmd

    nc = bacc.Bacc("TRN2", target_bir_lowering=False, num_devices=1)
    batch, depth = inputs["r_dense"].shape
    tables = [f"tbl_{i}" for i in range(inputs["ids"].shape[1])]
    order = w1_rows([inputs[name].shape[0] for name in tables], depth)
    laid = np.asarray(inputs["W_top1"])[np.array(order)]
    laid = laid.reshape(len(order) // P, P, -1).transpose(1, 0, 2)
    arrays, aps = {}, {}
    for name, value in {**inputs, "W_top1": laid}.items():
        a = np.ascontiguousarray(value)
        arrays[f"in_{name}"] = a
        aps[name] = nc.dram_tensor(f"in_{name}", a.shape, mybir.dt.from_np(a.dtype), kind="ExternalInput").ap()
    out = nc.dram_tensor("out_y", (batch, 1), F32, kind="ExternalOutput").ap()
    tower_program(nc, aps["r_dense"], aps["ids"], [aps[name] for name in tables], aps["W_top1"],
                  aps["b_top1"], aps["W_top2"], aps["b_top2"], aps["W_top3"], out)
    r = run_bass_kernel_spmd(nc, [arrays], core_ids=[0])
    return r.results[0]["out_y"]
```

```python
from contextlib import ExitStack

import concourse.bass as bass
from concourse import mybir

F32 = mybir.dt.float32
F32R = mybir.dt.float32r
I32 = mybir.dt.int32
ALU = mybir.AluOpType
ACT = mybir.ActivationFunctionType

P = 128
QUAD = 32
SLOTS = 28
ROWS_PER_PART = 8
CHOSEN_FROM = {0: 4, 1: 4, 2: 2}

PACK = [
    (0, 14, [(14, 1, 0), (14, 0, 1)]),
    (0, 7, [(2, 14, 14), (7, 1, 0), (7, 0, 1)]),
    (0, 4, [(4, 7, 7), (4, 1, 0), (3, 0, 1)]),
    (0, 2, [(4, 7, 7), (2, 1, 0), (2, 0, 1)]),
    (0, 1, [(4, 7, 7), (2, 2, 2)]),
    (4, 5, [(4, 7, 7), (2, 0, 1)]),
    (5, 6, [(4, 7, 7)]),
]
PACK_PARTS = [range(0, 1), range(1, 4), range(4, 7)]


def pack_order():
    order = []
    for n0, m0, dims in PACK:
        at = [(n0, m0)]
        for count, dn, dm in dims:
            at = [(n + i * dn, m + i * dm) for n, m in at for i in range(count)]
        order += at
    assert sorted(order) == [(n, m) for n in range(SLOTS) for m in range(n + 1, SLOTS)]
    return order


ORDER = """
I S0 L0 S1 J0 L1 J1 H0.0 T0.0 E0.0a H0.1 C0.0 H1.0 C0.1 H1.1 T0.1 E0a E0.1d S2 C1.0 J2 L2
C1.1 H2.0 T0.2 H2.1 E1a E0.2a C2.0 S3 J3 L3 C2.1 H3.0 T0.3 E2a H3.1 E0.3a C3.0 S4 J4 L4 C3.1
H4.0 T0.4 E3a H4.1 E0.4a C4.0 S5 J5 T0.5 L5 C4.1 E0.5a H5.0 X0.0 E4a S6 H5.1 X0.1 J6 L6 X0.2
H6.0 X0.3 T1.0 V0.0 C5.0 E1.0a V0.1 Q0.0d Q0.1a Q0.2a T1.1 H6.1 C5.1 E1.1a K0 E5a W0d S7
C6.0 J7 L7 A0.0 H7.0 A0.1 H7.1 R0.0 T1.2 R0.1 C6.1 E1.2d B0 E6a S8 J8 T1.3 L8 U0.0 T1.4 U0.1
E1.3a Y0 E1.4d C7.0 Z0a H8.0 C7.1 H8.1 T2.0 E7a S9 E2.0d X1.0 J9 L9 X1.1 H9.0 X1.2 X1.3 T2.1
V1.0 C8.0 E2.1a V1.1 Q1.0a C8.1 Q1.1a H9.1 Q1.2a T2.2 E8a K1 E2.2a C9.0 W1d C9.1 A1.0 E9a
A1.1 R1.0 T2.3 R1.1 T2.4 E2.3d B1 E2.4a X2.0 U1.0 U1.1 Y1 X2.1 Z1a X2.2 X2.3 T3.0 V2.0 T3.1
E3.0a V2.1 Q2.0d E3.1a Q2.1d Q2.2d K2 T3.2 W2a E3.2a A2.0 A2.1 R2.0 T3.3 R2.1 E3.3d T3.4 B2
E3.4a U2.0 U2.1 X3.0 X3.1 Y2 X3.2 X3.3 Z2a V3.0 Q3.0a V3.1 Q3.1d Q3.2a M k0 w0a k1 w1d k2
w2a m0 m1 m2 r0a r1d r2a r3d b u0a u1d Y3 Z3a
"""

STEP_NAMES = {
    "I": "ids", "S": "high", "L": "low", "J": "near", "H": "hot", "C": "choose", "T": "turn", "E": "empty",
    "X": "products", "V": "spread", "Q": "packing", "K": "pack", "W": "pairs", "A": "layer1",
    "R": "relu1", "B": "layer2", "U": "relu2", "Y": "layer3", "Z": "result",
    "M": "last_dense", "k": "last_pack", "w": "last_pairs", "m": "last_layer1", "r": "last_relu1",
    "b": "last_layer2", "u": "last_relu2",
}


def read_order(text):
    steps = []
    for word in text.split():
        who = {"a": "act", "d": "dve"}.get(word[-1])
        numbers = word[1:-1] if who else word[1:]
        steps.append((STEP_NAMES[word[0]], tuple(int(n) for n in numbers.split(".") if n), who))
    return steps


def slot_plan(table_rows):
    fit = [f for f, r in enumerate(table_rows) if r % ROWS_PER_PART == 0 and r // ROWS_PER_PART <= P]
    chosen, start = [], []
    for t, count in sorted(CHOSEN_FROM.items()):
        chosen += fit[len(chosen):len(chosen) + count]
        start += [t] * count
    assert len(chosen) == sum(CHOSEN_FROM.values())
    rest = [f for f in range(len(table_rows)) if f not in chosen]
    slots = [0] + [f + 1 for f in rest + chosen[::-1]]
    return slots, chosen, start


def w1_rows(table_rows, depth):
    slots, _, _ = slot_plan(table_rows)
    nf = len(slots)
    rows = []
    for n, m in pack_order():
        if max(n, m) < nf:
            a, b = sorted((slots[n], slots[m]))
            rows.append(a * (nf - 1) - a * (a - 1) // 2 + b - a - 1)
        else:
            rows.append(0)
    rows += [0] * (-len(rows) % P)
    return rows + [nf * (nf - 1) // 2 + d for d in range(depth)]


def tower_program(nc, r_dense, ids, tables, w1_laid, b_top1, W_top2, b_top2, W_top3, out):
    B, D = r_dense.shape
    NT = len(tables)
    TILES = B // P
    _, K1, H1 = w1_laid.shape
    H2 = W_top2.shape[1]
    M1, M2 = H1 // P, H2 // P
    NP = SLOTS * (SLOTS - 1) // 2
    PK = -(-NP // P)
    slots, chosen, start = slot_plan([t.shape[0] for t in tables])
    NF = len(slots)
    NCH = len(chosen)
    CR = tables[chosen[0]].shape[0] // ROWS_PER_PART
    CHUNKS = ROWS_PER_PART
    LEN = P * SLOTS
    assert D == P and NF < SLOTS and K1 == PK + 1 and M1 == 4 and M2 == 2

    def gathered(t):
        return NF - sum(1 for s in start if s <= t)

    def groups(t):
        return [list(range(a, min(a + 4, gathered(t)))) for a in range(0, gathered(t), 4)]

    STEPS = read_order(ORDER)
    turns = [n for name, n, _ in STEPS if name == "turn"]
    items = [n if name == "turn" else n[:1] for name, n, _ in STEPS
             if name == "turn" or (name == "choose" and n[1] == 0)]
    emptiers = [(n, who) for name, n, who in STEPS if name == "empty"]
    packers = [(n, who) for name, n, who in STEPS if name == "packing"]

    def count_of(jobs, n):
        who = dict(jobs)[n]
        own = [m for m, w in jobs if w == who]
        return who, own.index(n) + 1

    def items_of(t):
        return [n for n in items if (len(n) == 2 and n[0] == t) or (len(n) == 1 and start[n[0]] <= t)]

    def width(j):
        return (TILES - start[j]) * P

    with ExitStack() as ctx:
        def sb(name, shape, dt=F32):
            return ctx.enter_context(nc.sbuf_tensor("sb_" + name, shape, dt))

        def psum(name, shape):
            return ctx.enter_context(nc.psum_tensor("ps_" + name, shape, F32))

        def sem(name):
            return ctx.enter_context(nc.semaphore(name))

        TABLES_AHEAD = 3
        SPLITS = 2
        ONE_HOTS = 12
        ids_sb = sb("ids", [P, TILES, NT], I32)
        ids_f = sb("ids_f", [P, TILES, NT])
        ids_t = sb("ids_t", [NT, B], F32R)
        pick = sb("pick", [NT, NCH, P], F32R)
        int_minus_8p = sb("int_minus_8p", [P, 1], I32)
        minus_8p = sb("minus_8p", [P, 1])
        dense_sb = sb("dense", [P, TILES, D])
        rows = sb("rows", [P, sum(gathered(t) - 1 for t in range(TILES)), D])
        ident = sb("ident", [P, P])
        table = sb("table", [CR, TABLES_AHEAD, CHUNKS, D])
        table_hi = sb("table_hi", [CR, SPLITS, CHUNKS, D], F32R)
        table_lo = sb("table_lo", [CR, SPLITS, CHUNKS, D], F32R)
        id_less_8p = sb("id_less_8p", [CR, 2, B])
        one_hot = sb("one_hot", [CR, ONE_HOTS, B], F32R)
        feats = sb("feats", [P, TILES, LEN])
        spread = sb("spread", [P, NF, QUAD])
        packed = sb("packed", [P, PK * P])
        pairs = sb("pairs", [P, 2, PK, P])
        dense_t = sb("dense_t", [P, B])
        w1 = sb("w1", [P, K1, H1])
        w2 = sb("w2", [P, M1, H2])
        w3 = sb("w3", [P, M2])
        b1 = sb("b1", [P, M1])
        b2 = sb("b2", [P, M2])
        h1 = sb("h1", [P, M1, P])
        h2 = sb("h2", [P, M2, P])
        y_sb = sb("y", [1, B])

        turned_ps = psum("turned", [P, 2, 4 * P])
        ids_ps = psum("ids", [P, 2, 4 * P])
        prod_ps = psum("prod", [P, QUAD, QUAD])
        pack_ps = psum("pack", [P, 4, P])
        mlp_ps = psum("mlp", [P, 4, P])

        ids_in = sem("ids_in")
        dense_in = sem("dense_in")
        rows_in = {(t, q): sem(f"rows_in_{t}_{q}") for t in range(TILES) for q in range(len(groups(t)))}
        table_in = [sem(f"table_in_{r}") for r in range(TABLES_AHEAD)]
        weights_in = sem("weights_in")
        bias_in = sem("bias_in")
        ident_zero = sem("ident_zero")
        ident_ready = sem("ident_ready")
        int_minus_8p_ready = sem("int_minus_8p_ready")
        minus_8p_ready = sem("minus_8p_ready")
        picks_ready = sem("picks_ready")
        blanks_ready = sem("blanks_ready")
        ids_f_ready = sem("ids_f_ready")
        ids_turned = sem("ids_turned")
        ids_t_ready = sem("ids_t_ready")
        ids_spread = sem("ids_spread")
        near_ready = sem("near_ready")
        hi_ready = sem("hi_ready")
        lo_ready = sem("lo_ready")
        one_hot_ready = sem("one_hot_ready")
        one_hot_used = sem("one_hot_used")
        turned = sem("turned")
        emptied = {"dve": sem("emptied_by_dve"), "act": sem("emptied_by_act")}
        prods_ready = sem("prods_ready")
        spread_ready = sem("spread_ready")
        packed_by = {"dve": sem("packed_by_dve"), "act": sem("packed_by_act")}
        packs_turned = sem("packs_turned")
        pairs_ready = sem("pairs_ready")
        h1_summed = sem("h1_summed")
        h1_ready = sem("h1_ready")
        h2_summed = sem("h2_summed")
        h2_ready = sem("h2_ready")
        last_packed = [sem(f"last_packed_{k}") for k in range(PK)]
        last_pairs = [sem(f"last_pairs_{k}") for k in range(PK)]
        last_h1 = [sem(f"last_h1_{c}") for c in range(M1)]
        last_h2 = [sem(f"last_h2_{c}") for c in range(M2)]
        y_summed = sem("y_summed")
        y_ready = sem("y_ready")
        out_done = sem("out_done")

        block = ctx.enter_context(nc.Block())

        row_at = {}
        for t in range(TILES):
            for s in range(1, gathered(t)):
                row_at[t, s] = len(row_at)

        def feats_of(t):
            return feats[:, t, :].rearrange("p (b s) -> p s b", s=SLOTS)

        def empty(copy, wait, n, done_sem):
            bank = turned_ps[:, items.index(n) % 2, :]
            if len(n) == 2:
                t, q = n
                wait(turned, turns.index(n) + 1)
                g = groups(t)[q]
                if q == 0:
                    copy(dense_t[:, t * P:(t + 1) * P], bank[:, 0:P])
                done = copy(feats_of(t)[:, g[0]:g[-1] + 1, :],
                            bank[:, 0:len(g) * P].rearrange("p (s b) -> p s b", b=P))
            else:
                j, = n
                slot = NF - 1 - j
                wait(one_hot_used, CHUNKS * (j + 1))
                dst = feats[:, start[j]:TILES, :].rearrange("p t (b s) -> p t b s", s=SLOTS)[:, :, :, slot]
                done = copy(dst, bank[:, 0:width(j)].rearrange("p (t b) -> p t b", b=P))
            done.then_inc(done_sem, 1)

        def packing(copy, wait, t, part, done_sem):
            wait(spread_ready, 2 * t + (1 if part == 0 else 2))
            if t >= 1:
                wait(packs_turned, t)
            at = 0
            for r, (n0, m0, dims) in enumerate(PACK):
                sizes = [count for count, _, _ in dims]
                total, runs = 1, []
                for count in sizes[::-1]:
                    runs.insert(0, [total, count])
                    total *= count
                if r in PACK_PARTS[part]:
                    src, dst = spread[:, n0, m0:m0 + 1], packed[:, at:at + total]
                    done = copy(
                        bass.AP(dst.tensor, dst.offset, [list(dst.ap[0])] + runs),
                        bass.AP(src.tensor, src.offset, [list(src.ap[0])] + [
                            [dn * QUAD + dm, count] for count, dn, dm in dims]))
                at += total
            done.then_inc(done_sem, 1)

        def pairs_step(copy, wait, t):
            wait(packs_turned, t + 1)
            if t >= 2:
                wait(h1_summed, 2 * (t - 1))
            copy(pairs[:, t % 2, :, :], pack_ps[:, 0:PK, :]).then_inc(pairs_ready, 1)

        def result_step(copy, wait, t):
            wait(y_summed, t + 1)
            copy(y_sb[:, t * P:(t + 1) * P], mlp_ps[0:1, 3, :]).then_inc(y_ready, 1)

        def last_sum(c):
            return [mlp_ps[:, 0, :], ids_ps[:, 0, 0:P], ids_ps[:, 1, 0:P], turned_ps[:, 0, 0:P]][c]

        def last_pack(k):
            return [pack_ps[:, 0, :], turned_ps[:, 1, 0:P], prod_ps[:, 0:4, :].rearrange("p a b -> p (a b)")][k]

        def last_sum2(c):
            return [pack_ps[:, 3, :], turned_ps[:, 1, 3 * P:4 * P]][c]

        def last_pairs_step(copy, wait, k):
            wait(last_packed[k], 1)
            copy(pairs[:, (TILES - 1) % 2, k, :], last_pack(k)).then_inc(last_pairs[k], 1)

        def last_relu(me, dst, src, bias, done_sem):
            if me == "act":
                nc.scalar.activation(dst, src, ACT.Relu, bias=bias).then_inc(done_sem, 1)
            else:
                nc.vector.tensor_scalar(dst, src, bias, 0.0, ALU.add, ALU.max).then_inc(done_sem, 1)

        def either_engine(me, copy, wait, name, n, who):
            if who != me:
                return
            if name == "empty":
                empty(copy, wait, n, emptied[me])
            if name == "packing":
                packing(copy, wait, *n, packed_by[me])
            if name == "pairs":
                pairs_step(copy, wait, *n)
            if name == "result":
                result_step(copy, wait, *n)
            if name == "last_pairs":
                last_pairs_step(copy, wait, *n)
            if name == "last_relu1":
                c, = n
                wait(h1_summed, 2 * (TILES - 1) + c + 1)
                last_relu(me, h1[:, c, :], last_sum(c), b1[:, c:c + 1], last_h1[c])
            if name == "last_relu2":
                c, = n
                wait(h2_summed, 2 * (TILES - 1) + c + 1)
                last_relu(me, h2[:, c, :], last_sum2(c), b2[:, c:c + 1], last_h2[c])

        def h1_sum(c):
            return (mlp_ps if c < 2 else pack_ps)[:, c % 2, :]

        def h2_sum(c):
            return (mlp_ps if c < 1 else pack_ps)[:, 2, :]

        def load_table(q, j):
            src = tables[chosen[j]].rearrange("(p c) d -> p c d", c=ROWS_PER_PART)
            cut = CR // 16 * 16
            for a, b in ((0, cut), (cut, CR)):
                q.dma_start(table[a:b, j % TABLES_AHEAD, :, :], src[a:b]).then_inc(table_in[j % TABLES_AHEAD], 16)

        def load_weights(q):
            q.dma_start(w1[:, :, :], w1_laid).then_inc(weights_in, 16)
            q.dma_start(w2[:, :, :], W_top2.rearrange("(c p) n -> p c n", p=P)).then_inc(weights_in, 16)
            q.dma_start(w3[:, :], W_top3.rearrange("(c p) n -> p (c n)", p=P),
                         allow_slow_non_contiguous=True).then_inc(weights_in, 16)
            q.dma_start(b1[:, :], b_top1.rearrange("(c p) -> p c", p=P),
                         allow_slow_non_contiguous=True).then_inc(bias_in, 16)
            q.dma_start(b2[:, :], b_top2.rearrange("(c p) -> p c", p=P),
                         allow_slow_non_contiguous=True).then_inc(bias_in, 16)

        @block.sync
        def _(sp):
            sp.dma_start(ids_sb[:, :, :], ids.rearrange("(t p) f -> p t f", p=P)).then_inc(ids_in, 16)
            load_table(sp, 0)
            sp.dma_start(dense_sb[:, :, :], r_dense.rearrange("(t p) d -> p t d", p=P)).then_inc(dense_in, 16)
            for j in range(1, TABLES_AHEAD):
                load_table(sp, j)
            for j in range(TABLES_AHEAD, NCH):
                sp.wait_ge(lo_ready, j - TABLES_AHEAD + 1)
                load_table(sp, j)
                if j == TABLES_AHEAD:
                    load_weights(sp)
            sp.wait_ge(y_ready, TILES)
            sp.dma_start(out.rearrange("b n -> n b"), y_sb[:, :]).then_inc(out_done, 16)
            sp.wait_ge(out_done, 16)

        @block.gpsimd
        def _(pool):
            pool.memset(ident[:, :], 0.0).then_inc(ident_zero, 1)
            pool.iota(int_minus_8p[:, :], [[1, 1]], base=0, channel_multiplier=-ROWS_PER_PART).then_inc(int_minus_8p_ready, 1)
            pool.wait_ge(ident_zero, 1)
            pool.affine_select(out=ident[:, :], in_=ident[:, :], compare_op=ALU.not_equal, fill=1.0,
                               base=0, pattern=[[-1, P]], channel_multiplier=1).then_inc(ident_ready, 1)
            pool.wait_ge(ids_in, 16)
            for t in range(TILES):
                for q, group in enumerate(groups(t)):
                    for s in group:
                        if s > 0:
                            f = slots[s] - 1
                            pool.indirect_dma_start(
                                rows[:, row_at[t, s], :], None, tables[f],
                                bass.IndirectOffsetOnAxis(ids_sb[:, t, f:f + 1], 0)).then_inc(rows_in[t, q], 16)

        @block.vector
        def _(dve):
            dve.memset(prod_ps[:, :, 0:NF - 1], 0.0).then_inc(blanks_ready, 1)
            dve.memset(feats[:, :, :].rearrange("p t (b s) -> p t b s", s=SLOTS)[:, :, :, NF:SLOTS],
                       0.0).then_inc(blanks_ready, 1)
            dve.memset(packed[:, NP:PK * P], 0.0).then_inc(blanks_ready, 1)
            dve.memset(spread[:, NF - 1:NF, :], 0.0).then_inc(blanks_ready, 1)
            for name, n, who in STEPS:
                if name == "ids":
                    dve.wait_ge(ids_in, 16)
                    dve.tensor_copy(ids_f[:, :, :], ids_sb[:, :, :]).then_inc(ids_f_ready, 1)
                    dve.wait_ge(ids_turned, 1)
                    dve.tensor_copy(ids_t[:, :], ids_ps[0:NT, 0, :]).then_inc(ids_t_ready, 1)
                if name == "low":
                    j, = n
                    dve.wait_ge(hi_ready, j + 1)
                    if j >= SPLITS:
                        dve.wait_ge(one_hot_used, CHUNKS * (j - SPLITS + 1))
                    dve.tensor_tensor(table_lo[:, j % SPLITS, :, :], table[:, j % TABLES_AHEAD, :, :],
                                      table_hi[:, j % SPLITS, :, :], ALU.subtract).then_inc(lo_ready, 1)
                if name == "hot":
                    j, half = n
                    dve.wait_ge(near_ready, j + 1)
                    for c in range(half * CHUNKS // 2, (half + 1) * CHUNKS // 2):
                        at = j * CHUNKS + c
                        if at >= ONE_HOTS:
                            dve.wait_ge(one_hot_used, at - ONE_HOTS + 1)
                        dve.tensor_scalar(one_hot[:, at % ONE_HOTS, 0:width(j)], id_less_8p[:, j % 2, 0:width(j)],
                                          float(c), None, ALU.is_equal).then_inc(one_hot_ready, 1)
                if name == "spread":
                    t, half = n
                    if half == 0:
                        dve.wait_ge(prods_ready, t + 1)
                        if t >= 1:
                            for part in range(len(PACK_PARTS)):
                                by, count = count_of(packers, (t - 1, part))
                                dve.wait_ge(packed_by[by], count)
                    a, b = (0, SLOTS // 2) if half == 0 else (SLOTS // 2, NF - 1)
                    dve.transpose(spread[:, a:b, :], prod_ps[:, :, a:b].rearrange("p i n -> p n i")).then_inc(spread_ready, 1)
                either_engine("dve", dve.tensor_copy, dve.wait_ge, name, n, who)

        @block.scalar
        def _(act):
            act.wait_ge(int_minus_8p_ready, 1)
            act.copy(minus_8p[:, :], int_minus_8p[:, :]).then_inc(minus_8p_ready, 1)
            act.wait_ge(ident_ready, 1)
            for j in range(NCH):
                act.copy(pick[:, j, :], ident[0:NT, chosen[j]:chosen[j] + 1].to_broadcast([NT, P])).then_inc(picks_ready, 1)
            for name, n, who in STEPS:
                if name == "high":
                    j, = n
                    act.wait_ge(table_in[j % TABLES_AHEAD], 32 * (j // TABLES_AHEAD + 1))
                    if j >= SPLITS:
                        act.wait_ge(one_hot_used, CHUNKS * (j - SPLITS + 1))
                    act.copy(table_hi[:, j % SPLITS, :, :], table[:, j % TABLES_AHEAD, :, :]).then_inc(hi_ready, 1)
                if name == "near":
                    j, = n
                    act.wait_ge(ids_spread, j + 1)
                    if j == 0:
                        act.wait_ge(minus_8p_ready, 1)
                    act.activation(id_less_8p[:, j % 2, 0:width(j)], ids_ps[0:CR, j % 2, 0:width(j)],
                                   ACT.Identity, bias=minus_8p[0:CR, :]).then_inc(near_ready, 1)
                if name == "relu1":
                    t, half = n
                    if t == 0 and half == 0:
                        act.wait_ge(bias_in, 32)
                    act.wait_ge(h1_summed, 2 * t + half + 1)
                    for c in range(2):
                        unit = 2 * half + c
                        done = act.activation(h1[:, unit, :], h1_sum(unit), ACT.Relu, bias=b1[:, unit:unit + 1])
                    done.then_inc(h1_ready, 1)
                if name == "relu2":
                    t, c = n
                    act.wait_ge(h2_summed, 2 * t + c + 1)
                    act.activation(h2[:, c, :], h2_sum(c), ACT.Relu, bias=b2[:, c:c + 1]).then_inc(h2_ready, 1)
                either_engine("act", act.copy, act.wait_ge, name, n, who)

        @block.tensor
        def _(pe):
            def bank_free(i):
                if i >= 2:
                    by, count = count_of(emptiers, items[i - 2])
                    pe.wait_ge(emptied[by], count)

            def spread_ids(j):
                w = width(j)
                pe.matmul(ids_ps[:, j % 2, 0:w], pick[:, j, :], ids_t[:, B - w:B],
                          start=True, stop=True).then_inc(ids_spread, 1)

            def layer2_part(c, ks):
                for k in ks:
                    done = pe.matmul(h2_sum(c), w2[:, k, c * P:(c + 1) * P], h1[:, k, :],
                                     start=(k == 0), stop=(k == M1 - 1))
                return done

            for name, n, _ in STEPS:
                if name == "ids":
                    pe.wait_ge(ident_ready, 1)
                    pe.wait_ge(ids_f_ready, 1)
                    for t in range(TILES):
                        done = pe.transpose(ids_ps[0:NT, 0, t * P:(t + 1) * P], ids_f[:, t, :], ident[:, :])
                    done.then_inc(ids_turned, 1)
                    pe.wait_ge(ids_t_ready, 1)
                    pe.wait_ge(picks_ready, NCH)
                    pe.wait_ge(blanks_ready, 4)
                    spread_ids(0)
                    spread_ids(1)
                if name == "turn":
                    t, q = n
                    i = items.index(n)
                    group = groups(t)[q]
                    if q == 0:
                        pe.wait_ge(dense_in, 16)
                    bank_free(i)
                    pe.wait_ge(rows_in[t, q], 16 * len([s for s in group if s > 0]))
                    for k, s in enumerate(group):
                        src = dense_sb[:, t, :] if s == 0 else rows[:, row_at[t, s], :]
                        done = pe.transpose(turned_ps[:, i % 2, k * P:(k + 1) * P], src, ident[:, :])
                    done.then_inc(turned, 1)
                if name == "choose":
                    j, half = n
                    i = items.index((j,))
                    w = width(j)
                    if half == 0:
                        bank_free(i)
                        pe.wait_ge(lo_ready, j + 1)
                    for c in range(half * CHUNKS // 2, (half + 1) * CHUNKS // 2):
                        at = j * CHUNKS + c
                        pe.wait_ge(one_hot_ready, at + 1)
                        hot = one_hot[:, at % ONE_HOTS, 0:w]
                        pe.matmul(turned_ps[:, i % 2, 0:w], table_hi[:, j % SPLITS, c, :], hot, start=(c == 0), stop=False)
                        pe.matmul(turned_ps[:, i % 2, 0:w], table_lo[:, j % SPLITS, c, :], hot,
                                  start=False, stop=(c == CHUNKS - 1)).then_inc(one_hot_used, 1)
                    if half == 1 and j + 2 < NCH:
                        spread_ids(j + 2)
                if name == "products":
                    t, part = n
                    if part == 0:
                        counts = {}
                        for item in items_of(t):
                            by, count = count_of(emptiers, item)
                            counts[by] = max(count, counts.get(by, 0))
                        for by, count in sorted(counts.items()):
                            pe.wait_ge(emptied[by], count)
                        if t >= 1:
                            pe.wait_ge(spread_ready, 2 * t)
                    for i in range(part * QUAD // 4, (part + 1) * QUAD // 4):
                        for quad in range(P // QUAD):
                            at = (quad * QUAD + i) * SLOTS
                            done = pe.matmul(prod_ps[quad * QUAD:quad * QUAD + SLOTS, i, 0:NF - 1],
                                             feats[:, t, at:at + SLOTS], feats[:, t, at:at + NF - 1],
                                             start=True, stop=True)
                    if part == 3:
                        done.then_inc(prods_ready, 1)
                if name == "pack":
                    t, = n
                    for part in range(len(PACK_PARTS)):
                        by, count = count_of(packers, (t, part))
                        pe.wait_ge(packed_by[by], count)
                    if t >= 1:
                        pe.wait_ge(h2_ready, 2 * t)
                    for k in range(PK):
                        done = pe.transpose(pack_ps[:, k, :], packed[:, k * P:(k + 1) * P], ident[:, :])
                    done.then_inc(packs_turned, 1)
                if name == "layer1":
                    t, half = n
                    pe.wait_ge(pairs_ready, t + 1)
                    if half == 0:
                        if t == 0:
                            pe.wait_ge(weights_in, 48)
                        else:
                            pe.wait_ge(y_ready, t)
                    for c in range(2 * half, 2 * half + 2):
                        for k in range(K1):
                            part = pairs[:, t % 2, k, :] if k < PK else dense_t[:, t * P:(t + 1) * P]
                            done = pe.matmul(h1_sum(c), w1[:, k, c * P:(c + 1) * P], part,
                                             start=(k == 0), stop=(k == K1 - 1))
                    done.then_inc(h1_summed, 1)
                if name == "layer2":
                    t, = n
                    pe.wait_ge(h1_ready, 2 * t + 1)
                    layer2_part(0, range(0, 2))
                    pe.wait_ge(h1_ready, 2 * t + 2)
                    layer2_part(0, range(2, M1)).then_inc(h2_summed, 1)
                    layer2_part(1, range(M1)).then_inc(h2_summed, 1)
                if name == "last_dense":
                    pe.wait_ge(y_ready, TILES - 1)
                    for c in range(M1):
                        pe.matmul(last_sum(c), w1[:, PK, c * P:(c + 1) * P],
                                  dense_t[:, (TILES - 1) * P:TILES * P], start=True, stop=False)
                if name == "last_pack":
                    k, = n
                    for part in range(1 if k == 0 else len(PACK_PARTS)):
                        by, count = count_of(packers, (TILES - 1, part))
                        pe.wait_ge(packed_by[by], count)
                    if k == 0:
                        pe.wait_ge(h2_ready, 2 * (TILES - 1))
                    pe.transpose(last_pack(k), packed[:, k * P:(k + 1) * P], ident[:, :]).then_inc(last_packed[k], 1)
                if name == "last_layer1":
                    k, = n
                    pe.wait_ge(last_pairs[k], 1)
                    for c in range(M1):
                        done = pe.matmul(last_sum(c), w1[:, k, c * P:(c + 1) * P], pairs[:, (TILES - 1) % 2, k, :],
                                         start=False, stop=(k == PK - 1))
                        if k == PK - 1:
                            done.then_inc(h1_summed, 1)
                if name == "last_layer2":
                    for k in range(M1):
                        pe.wait_ge(last_h1[k], 1)
                        for c in range(M2):
                            done = pe.matmul(last_sum2(c), w2[:, k, c * P:(c + 1) * P], h1[:, k, :],
                                             start=(k == 0), stop=(k == M1 - 1))
                            if k == M1 - 1:
                                done.then_inc(h2_summed, 1)
                if name == "layer3":
                    t, = n
                    for k in range(M2):
                        if t == TILES - 1:
                            pe.wait_ge(last_h2[k], 1)
                        else:
                            pe.wait_ge(h2_ready, 2 * t + k + 1)
                        done = pe.matmul(mlp_ps[0:1, 3, :], w3[:, k:k + 1], h2[:, k, :],
                                         start=(k == 0), stop=(k == M2 - 1))
                    done.then_inc(y_summed, 1)


def kernel(**inputs):
    import numpy as np
    import concourse.bacc as bacc
    from concourse.bass_utils import run_bass_kernel_spmd

    nc = bacc.Bacc("TRN2", target_bir_lowering=False, num_devices=1)
    batch, depth = inputs["r_dense"].shape
    tables = [f"tbl_{i}" for i in range(inputs["ids"].shape[1])]
    order = w1_rows([inputs[name].shape[0] for name in tables], depth)
    laid = np.asarray(inputs["W_top1"])[np.array(order)]
    laid = laid.reshape(len(order) // P, P, -1).transpose(1, 0, 2)
    arrays, aps = {}, {}
    for name, value in {**inputs, "W_top1": laid}.items():
        a = np.ascontiguousarray(value)
        arrays[f"in_{name}"] = a
        aps[name] = nc.dram_tensor(f"in_{name}", a.shape, mybir.dt.from_np(a.dtype), kind="ExternalInput").ap()
    out = nc.dram_tensor("out_y", (batch, 1), F32, kind="ExternalOutput").ap()
    tower_program(nc, aps["r_dense"], aps["ids"], [aps[name] for name in tables], aps["W_top1"],
                  aps["b_top1"], aps["W_top2"], aps["b_top2"], aps["W_top3"], out)
    r = run_bass_kernel_spmd(nc, [arrays], core_ids=[0])
    return r.results[0]["out_y"]
```
